# Optimizing a Trainium2 kernel written in Bass

```python
import numpy as np
import jax
import jax.numpy as jnp

def _softmax(x, axis=-1):
    return jax.nn.softmax(x, axis=axis)

def _gelu(x):
    return jax.nn.gelu(x, approximate=True)

def _silu(x):
    return jax.nn.silu(x)

def _sigmoid(x):
    return jax.nn.sigmoid(x)

def _layernorm(x, axis=-1, eps=1e-05):
    m = jnp.mean(x, axis=axis, keepdims=True)
    v = jnp.var(x, axis=axis, keepdims=True)
    return (x - m) / jnp.sqrt(v + eps)

def _scatter_add(tgt, idx, src, axis=0):
    return tgt.at[idx].add(src)

def _segment_sum(src, seg, n):
    return jax.ops.segment_sum(src, seg, n)
kernel_name = 'mk_rec_standalone_d1_rec_r8_07e430'

def setup_inputs(seed: int=0):
    np.random.seed(seed)
    _w = jnp.asarray

    def _rec_inputs():
        import jax
        import jax.numpy as jnp
        _rk = jax.random.key(seed)
        r_dense_x = -0.00142785 + 1.00275 * jax.random.normal(jax.random.fold_in(_rk, 1), (2048, 13), jnp.float32)
        r_sparse_idx = jax.random.randint(jax.random.fold_in(_rk, 2), (2048, 26, 4), 0, 12500, jnp.int32)
        return (r_dense_x, r_sparse_idx)
    r_dense_x, r_sparse_idx = _rec_inputs()

    def _L0_rec_setup():
        import jax, jax.numpy as jnp
        import numpy as np
        B, T, L = (512, 26, 4)
        N_ROWS, M = (12500, 64)
        LN_BOT = [13, 512, 256, 64]
        LN_TOP = [415, 512, 256, 1]

        def _mlp_params(key, ln):
            Ws, bs = ([], [])
            for i in range(len(ln) - 1):
                n, m = (ln[i], ln[i + 1])
                key, k1, k2 = jax.random.split(key, 3)
                Ws.append(jax.random.normal(k1, (m, n), jnp.float32) * np.sqrt(2.0 / (m + n)))
                bs.append(jax.random.normal(k2, (m,), jnp.float32) * np.sqrt(1.0 / m))
            return (Ws, bs)

        def _dlrm_forward(dense_x, sparse_idx, emb_tables, bot, top):
            x = dense_x
            for W, b in bot:
                x = jax.nn.relu(x @ W.T + b)
            E = jax.vmap(lambda tab, ix: tab[ix].sum(axis=1), in_axes=(0, 1), out_axes=1)(emb_tables, sparse_idx)
            Tcat = jnp.concatenate([x[:, None, :], E], axis=1)
            Z = jnp.einsum('bim,bjm->bij', Tcat, Tcat)
            li, lj = np.tril_indices(T + 1, k=-1)
            Zflat = Z[:, li, lj]
            R = jnp.concatenate([x, Zflat], axis=1)
            h = R
            for i, (W, b) in enumerate(top):
                h = h @ W.T + b
                h = jax.nn.sigmoid(h) if i == len(top) - 1 else jax.nn.relu(h)
            return h
        key = jax.random.key(seed)
        k_dense, k_idx, k_emb, k_bot, k_top = jax.random.split(key, 5)
        dense_x = jax.random.normal(k_dense, (B, LN_BOT[0]), jnp.float32)
        sparse_idx = jax.random.randint(k_idx, (B, T, L), 0, N_ROWS, jnp.int64 if jax.config.jax_enable_x64 else jnp.int32)
        bound = np.sqrt(1.0 / N_ROWS)
        emb_tables = jax.random.uniform(k_emb, (T, N_ROWS, M), jnp.float32, -bound, bound)
        bw, bb = _mlp_params(k_bot, LN_BOT)
        tw, tb = _mlp_params(k_top, LN_TOP)
        return {'dense_x': dense_x, 'sparse_idx': sparse_idx, 'emb_tables': emb_tables, 'bot_W0': bw[0], 'bot_b0': bb[0], 'bot_W1': bw[1], 'bot_b1': bb[1], 'bot_W2': bw[2], 'bot_b2': bb[2], 'top_W0': tw[0], 'top_b0': tb[0], 'top_W1': tw[1], 'top_b1': tb[1], 'top_W2': tw[2], 'top_b2': tb[2]}
    _L0_rec_all = _L0_rec_setup()
    _L0_rec_in = {k: v for k, v in _L0_rec_all.items() if k in ('emb_tables', 'bot_W0', 'bot_b0', 'bot_W1', 'bot_b1', 'bot_W2', 'bot_b2', 'top_W0', 'top_b0', 'top_W1', 'top_b1', 'top_W2', 'top_b2')}
    del _L0_rec_all
    return {'r_dense_x': r_dense_x, 'r_sparse_idx': r_sparse_idx, 'L0_rec_emb_tables': _L0_rec_in['emb_tables'], 'L0_rec_bot_W0': _L0_rec_in['bot_W0'], 'L0_rec_bot_b0': _L0_rec_in['bot_b0'], 'L0_rec_bot_W1': _L0_rec_in['bot_W1'], 'L0_rec_bot_b1': _L0_rec_in['bot_b1'], 'L0_rec_bot_W2': _L0_rec_in['bot_W2'], 'L0_rec_bot_b2': _L0_rec_in['bot_b2'], 'L0_rec_top_W0': _L0_rec_in['top_W0'], 'L0_rec_top_b0': _L0_rec_in['top_b0'], 'L0_rec_top_W1': _L0_rec_in['top_W1'], 'L0_rec_top_b1': _L0_rec_in['top_b1'], 'L0_rec_top_W2': _L0_rec_in['top_W2'], 'L0_rec_top_b2': _L0_rec_in['top_b2']}

def reference(r_dense_x, r_sparse_idx, L0_rec_emb_tables, L0_rec_bot_W0, L0_rec_bot_b0, L0_rec_bot_W1, L0_rec_bot_b1, L0_rec_bot_W2, L0_rec_bot_b2, L0_rec_top_W0, L0_rec_top_b0, L0_rec_top_W1, L0_rec_top_b1, L0_rec_top_W2, L0_rec_top_b2):
    import jax
    import jax.numpy as jnp

    def _L0_rec_ref(dense_x, sparse_idx, emb_tables, bot_W0, bot_b0, bot_W1, bot_b1, bot_W2, bot_b2, top_W0, top_b0, top_W1, top_b1, top_W2, top_b2):
        import jax, jax.numpy as jnp
        import numpy as np
        B, T, L = (512, 26, 4)
        N_ROWS, M = (12500, 64)
        LN_BOT = [13, 512, 256, 64]
        LN_TOP = [415, 512, 256, 1]

        def _mlp_params(key, ln):
            Ws, bs = ([], [])
            for i in range(len(ln) - 1):
                n, m = (ln[i], ln[i + 1])
                key, k1, k2 = jax.random.split(key, 3)
                Ws.append(jax.random.normal(k1, (m, n), jnp.float32) * np.sqrt(2.0 / (m + n)))
                bs.append(jax.random.normal(k2, (m,), jnp.float32) * np.sqrt(1.0 / m))
            return (Ws, bs)

        def _dlrm_forward(dense_x, sparse_idx, emb_tables, bot, top):
            x = dense_x
            for W, b in bot:
                x = jax.nn.relu(x @ W.T + b)
            E = jax.vmap(lambda tab, ix: tab[ix].sum(axis=1), in_axes=(0, 1), out_axes=1)(emb_tables, sparse_idx)
            Tcat = jnp.concatenate([x[:, None, :], E], axis=1)
            Z = jnp.einsum('bim,bjm->bij', Tcat, Tcat)
            li, lj = np.tril_indices(T + 1, k=-1)
            Zflat = Z[:, li, lj]
            R = jnp.concatenate([x, Zflat], axis=1)
            h = R
            for i, (W, b) in enumerate(top):
                h = h @ W.T + b
                h = jax.nn.sigmoid(h) if i == len(top) - 1 else jax.nn.relu(h)
            return h
        bot = [(bot_W0, bot_b0), (bot_W1, bot_b1), (bot_W2, bot_b2)]
        top = [(top_W0, top_b0), (top_W1, top_b1), (top_W2, top_b2)]
        return _dlrm_forward(dense_x, sparse_idx, emb_tables, bot, top)
    y = _L0_rec_ref(r_dense_x, r_sparse_idx, L0_rec_emb_tables, L0_rec_bot_W0, L0_rec_bot_b0, L0_rec_bot_W1, L0_rec_bot_b1, L0_rec_bot_W2, L0_rec_bot_b2, L0_rec_top_W0, L0_rec_top_b0, L0_rec_top_W1, L0_rec_top_b1, L0_rec_top_W2, L0_rec_top_b2)
    return y

_drawn_inputs = setup_inputs


def setup_inputs(seed=0):
    import zlib

    import numpy as np

    out = dict(_drawn_inputs(seed))
    spreads = {}
    factors = {'r_dense_x': 8.0,
     'L0_rec_emb_tables': 8.0,
     'L0_rec_bot_W0': 8.0,
     'L0_rec_bot_b0': 8.0,
     'L0_rec_bot_W1': 6.254,
     'L0_rec_bot_b1': 8.0,
     'L0_rec_bot_W2': 8.0,
     'L0_rec_bot_b2': 28.516,
     'L0_rec_top_W0': 7.646,
     'L0_rec_top_b0': 200.0,
     'L0_rec_top_W1': 4.886,
     'L0_rec_top_b1': 200.0,
     'L0_rec_top_W2': 5.464}
    for name, (base, spread) in spreads.items():
        noise = np.random.default_rng([zlib.crc32(name.encode()), seed]).standard_normal(out[name].shape)
        drawn = base * np.exp(spread * noise) if base else spread * noise
        out[name] = jnp.asarray(drawn.astype(out[name].dtype))
    for name, factor in factors.items():
        out[name] = (out[name] * factor).astype(out[name].dtype)
    return out
```

```python
from contextlib import ExitStack

import concourse.bass as bass
from concourse import mybir

F32 = mybir.dt.float32
I32 = mybir.dt.int32
ALU = mybir.AluOpType
ACT = mybir.ActivationFunctionType

P = 128
Q = 32
ACT_SAMPLES, DVE_SAMPLES = (0, 1), (2, 3)


def dlrm_kernel(nc, dense, sparse_idx, emb, bw0, bb0, bw1, bb1, bw2, bb2, tw0x, tw0z, tb0, tw1, tb1, tw2, tb2, out):
    dense_in, steps, lanes = dense.shape
    samples, tables, lookups = sparse_idx.shape
    rows_per_table = emb.shape[1]
    dim = emb.shape[2]
    assert lanes == Q and lookups * lanes == P and steps * lanes == samples
    vectors = tables + 1
    pairs = tables // 2
    assert 2 * dim == P and tables % 2 == 0 and vectors <= Q
    h1, h2 = bw0.shape[1], bw1.shape[2]
    t1, t2 = tw0x.shape[1], tw1.shape[2]
    kb1, kb2, kt1, kt2 = h1 // P, h2 // P, t1 // P, t2 // P
    ring = 4
    groups = steps // ring
    wide = ring * lanes
    column_sets = -(-vectors // 4)
    quads = lanes // 4

    emb_rows = emb.rearrange("t r d -> (t r) d")
    idx_by_lane = sparse_idx.rearrange("(p u) t l -> p (u t l)", u=steps)
    per_step = tables * lookups

    with ExitStack() as ctx:
        def sb(name, shape, dt=F32):
            return ctx.enter_context(nc.sbuf_tensor(name, shape, dt))

        def ps(name, shape):
            return ctx.enter_context(nc.psum_tensor(name, shape, F32))

        def sem(name):
            return ctx.enter_context(nc.semaphore(name))

        raw_idx = sb("raw_idx", [P, steps * per_step], I32)
        row_ids = sb("row_ids", [P, ring, tables], I32)
        table_base_int = sb("table_base_int", [P, tables], I32)
        table_base = sb("table_base", [P, tables])
        fetched = sb("fetched", [P, ring, tables, dim])
        lane_sum = sb("lane_sum", [P, lanes])
        vec = sb("vec", [dim + 1, ring, lanes, Q])
        z = sb("z", [P, column_sets, ring, lanes])
        dense_sb = sb("dense_sb", [dense_in + 1, steps * lanes])
        bw0_sb = sb("bw0_sb", [dense_in + 1, h1])
        bw1_sb = sb("bw1_sb", [P, kb1, h2])
        bb1_sb = sb("bb1_sb", [P, kb2])
        bw2_sb = sb("bw2_sb", [P, kb2, dim])
        bb2_sb = sb("bb2_sb", [dim, 1])
        bh1 = sb("bh1", [P, kb1, wide])
        bh2 = sb("bh2", [P, kb2, wide])
        tw0x_sb = sb("tw0x_sb", [dim + 1, t1])
        tw0z_sb = sb("tw0z_sb", [P, column_sets, t1])
        tw1_sb = sb("tw1_sb", [P, kt1, t2])
        tb1_sb = sb("tb1_sb", [P, kt2])
        tw2_sb = sb("tw2_sb", [P, kt2, 1])
        tb2_sb = sb("tb2_sb", [1, 1])
        th1 = sb("th1", [P, kt1, wide])
        th2 = sb("th2", [P, kt2, wide])
        y = sb("y", [1, lanes, steps])

        sums_ps = [ps(f"sums_ps{i}", [P, pairs, lanes]) for i in range(2)]
        z_ps = ps("z_ps", [P, quads, P])
        top1_ps = ps("top1_ps", [P, kt1, wide])
        top2_ps = ps("top2_ps", [P, kt2 + 1, wide])
        bot1_ps = ps("bot1_ps", [P, kb1, wide])
        bot2_ps = ps("bot2_ps", [P, kb2 + 1, wide])

        idx_first = sem("idx_first")
        idx_rest = sem("idx_rest")
        ones_set = sem("ones_set")
        bot_loaded = sem("bot_loaded")
        top_loaded = sem("top_loaded")
        base_made = sem("base_made")
        sum_cleared = sem("sum_cleared")
        sum_made = sem("sum_made")
        vec_set = sem("vec_set")
        ids_ready = sem("ids_ready")
        gathered = [sem(f"gathered{i}") for i in range(ring)]
        summed = sem("summed")
        even_copied = sem("even_copied")
        odd_copied = sem("odd_copied")
        bot1_done = sem("bot1_done")
        bot1_relu = sem("bot1_relu")
        bot2_done = sem("bot2_done")
        bot2_relu = sem("bot2_relu")
        bot3_done = sem("bot3_done")
        x_ready = sem("x_ready")
        z_done = sem("z_done")
        z_copied_act = sem("z_copied_act")
        z_copied_dve = sem("z_copied_dve")
        top1_done = sem("top1_done")
        top1_relu = sem("top1_relu")
        top2_done = sem("top2_done")
        top2_relu = sem("top2_relu")
        top3_done = sem("top3_done")
        y_ready = sem("y_ready")
        stored = sem("stored")

        block = ctx.enter_context(nc.Block())
        first = ring * per_step

        def z_from(r, q):
            return z_ps[r * Q:(r + 1) * Q, :, r * Q + q:r * Q + 4 * column_sets:4].rearrange("p n j -> p j n")

        def z_to(s, r, q):
            return z[q * Q:(q + 1) * Q, :, s, r:lanes:4]

        @block.sync
        def _(sp):
            for q in range(4):
                sp.dma_start(raw_idx[q * Q:(q + 1) * Q, 0:first], idx_by_lane[:, 0:first]).then_inc(idx_first, 16)
            for q in range(4):
                sp.dma_start(raw_idx[q * Q:(q + 1) * Q, first:], idx_by_lane[:, first:]).then_inc(idx_rest, 16)
            sp.wait_ge(y_ready, groups)
            sp.dma_start(out.rearrange("(a n) c -> a (n c)", a=1), y.rearrange("a p u -> a (p u)")).then_inc(stored, 16)
            sp.wait_ge(stored, 16)

        @block.gpsimd
        def _(pool):
            pool.iota(table_base_int[:, :], pattern=[[rows_per_table, tables]], base=0, channel_multiplier=0).then_inc(base_made, 1)
            pool.wait_ge(base_made, 1)
            pool.tensor_copy(table_base[:, :], table_base_int[:, :]).then_inc(base_made, 1)
            pool.memset(lane_sum[:, :], 0.0).then_inc(sum_cleared, 1)
            pool.wait_ge(sum_cleared, 1)
            for q in range(4):
                part = lane_sum[q * Q:(q + 1) * Q, :]
                pool.affine_select(out=part, in_=part, compare_op=ALU.not_equal, fill=1.0, base=0,
                                   pattern=[[-1, lanes]], channel_multiplier=1).then_inc(sum_made, 1)

            def gather_step(s):
                for t in range(tables):
                    pool.indirect_dma_start(
                        out=fetched[:, s, t, :], out_offset=None, in_=emb_rows,
                        in_offset=bass.IndirectOffsetOnAxis(ap=row_ids[:, s, t:t + 1], axis=0),
                    ).then_inc(gathered[s], 16)

            pool.wait_ge(sum_made, 4)
            for s in range(ring):
                pool.wait_ge(ids_ready, s + 1)
                gather_step(s)
            due = [pool.alloc_register("due_even"), pool.alloc_register("due_odd")]
            pool.reg_mov(due[0], ring + 1)
            with pool.Fori(1, groups):
                for s in range(ring):
                    pool.wait_ge(ids_ready, due[s % 2])
                    pool.reg_add(due[1 - s % 2], due[s % 2], 1)
                    gather_step(s)

        @block.scalar
        def _(act):
            act.dma_start(bw0_sb[0:dense_in, :], bw0).then_inc(bot_loaded, 16)
            act.dma_start(bw0_sb[dense_in:dense_in + 1, :], bb0.rearrange("(a n) -> a n", a=1)).then_inc(bot_loaded, 16)
            act.wait_ge(ones_set, 1)
            act.dma_start(dense_sb[0:dense_in, :], dense.rearrange("k u p -> k (u p)")).then_inc(bot_loaded, 16)
            act.dma_start(bw1_sb[:, :, :], bw1).then_inc(bot_loaded, 16)
            act.dma_start(bb1_sb[:, :], bb1).then_inc(bot_loaded, 16)
            act.dma_start(bw2_sb[:, :, :], bw2).then_inc(bot_loaded, 16)
            act.dma_start(bb2_sb[:, :], bb2).then_inc(bot_loaded, 16)
            act.dma_start(tw0x_sb[0:dim, :], tw0x).then_inc(top_loaded, 16)
            act.dma_start(tw0x_sb[dim:dim + 1, :], tb0.rearrange("(a n) -> a n", a=1)).then_inc(top_loaded, 16)
            act.dma_start(tw0z_sb[:, :, :], tw0z).then_inc(top_loaded, 16)
            act.dma_start(tw1_sb[:, :, :], tw1).then_inc(top_loaded, 16)
            act.dma_start(tb1_sb[:, :], tb1).then_inc(top_loaded, 16)
            act.dma_start(tw2_sb[:, :, :], tw2).then_inc(top_loaded, 16)
            act.dma_start(tb2_sb[:, :], tb2.rearrange("(a n) -> a n", a=1)).then_inc(top_loaded, 16)
            act.wait_ge(top_loaded, 16 * 7)

            def step(u, s):
                act.wait_ge(summed, u + 1)
                act.activation(vec[0:dim, s, :, 2:vectors:2].rearrange("p b k -> p k b"),
                               sums_ps[s % 2][dim:P, :, :], ACT.Copy).then_inc(odd_copied, 1)
                act.wait_ge(z_done, u + 1)
                for r in ACT_SAMPLES:
                    for q in range(4):
                        last = act.activation(z_to(s, r, q), z_from(r, q), ACT.Copy)
                last.then_inc(z_copied_act, 1)

            with act.Fori(0, groups) as g:
                for s in range(ring):
                    step(ring * g + s, s)
                act.wait_ge(top3_done, g + 1)
                act.activation(y[0:1, :, bass.ds(ring * g, ring)].rearrange("a b s -> a s b"),
                               top2_ps[0:1, kt2, :].rearrange("a (s b) -> a s b", s=ring),
                               ACT.Sigmoid, bias=tb2_sb[0:1, 0:1]).then_inc(y_ready, 1)

        @block.vector
        def _(dve):
            dve.memset(dense_sb[:, :], 1.0).then_inc(ones_set, 1)

            def make_ids(column, s):
                for l in range(lookups):
                    part = slice(l * Q, (l + 1) * Q)
                    picked = raw_idx[part, bass.ds(column, per_step)].rearrange("p (t l) -> p t l", l=lookups)[:, :, l]
                    last = dve.tensor_tensor(row_ids[part, s, :], picked, table_base[part, :], ALU.add)
                last.then_inc(ids_ready, 1)

            dve.wait_ge(base_made, 2)
            dve.wait_ge(idx_first, 16 * 4)
            for s in range(ring):
                make_ids(s * per_step, s)
            dve.memset(vec[0:dim, :, :, vectors:Q], 0.0)
            dve.memset(vec[dim:dim + 1, :, :, 0], 1.0).then_inc(vec_set, 1)
            dve.wait_ge(bot_loaded, 16 * 7)
            dve.wait_ge(top_loaded, 16 * 7)
            dve.wait_ge(idx_rest, 16 * 4)

            def relus_bottom(g):
                dve.wait_ge(bot1_done, g + 1)
                dve.tensor_scalar(bh1[:, :, :], bot1_ps[:, :, :], 0.0, None, ALU.max).then_inc(bot1_relu, 1)
                dve.wait_ge(bot2_done, g + 1)
                for m in range(kb2):
                    last = dve.tensor_scalar(bh2[:, m, :], bot2_ps[:, m, :], bb1_sb[:, m:m + 1], 0.0, ALU.add, ALU.max)
                last.then_inc(bot2_relu, 1)
                dve.wait_ge(bot3_done, g + 1)
                dve.tensor_scalar(vec[0:dim, :, :, 0], bot2_ps[0:dim, kb2, :].rearrange("p (s b) -> p s b", s=ring),
                                  bb2_sb[:, 0:1], 0.0, ALU.add, ALU.max).then_inc(x_ready, 1)

            def step(u, s, next_column):
                dve.wait_ge(summed, u + 1)
                dve.tensor_copy(vec[0:dim, s, :, 1:vectors:2].rearrange("p b k -> p k b"),
                                sums_ps[s % 2][0:dim, :, :]).then_inc(even_copied, 1)
                if next_column is not None:
                    make_ids(next_column, s)
                dve.wait_ge(z_done, u + 1)
                for r in DVE_SAMPLES:
                    for q in range(4):
                        last = dve.tensor_copy(z_to(s, r, q), z_from(r, q))
                last.then_inc(z_copied_dve, 1)

            def relus_top(g):
                dve.wait_ge(top1_done, g + 1)
                dve.tensor_scalar(th1[:, :, :], top1_ps[:, :, :], 0.0, None, ALU.max).then_inc(top1_relu, 1)
                dve.wait_ge(top2_done, g + 1)
                for m in range(kt2):
                    last = dve.tensor_scalar(th2[:, m, :], top2_ps[:, m, :], tb1_sb[:, m:m + 1], 0.0, ALU.add, ALU.max)
                last.then_inc(top2_relu, 1)

            with dve.Fori(0, groups - 1) as g:
                relus_bottom(g)
                for s in range(ring):
                    u = ring * g + s
                    step(u, s, (u + ring) * per_step)
                relus_top(g)
            relus_bottom(groups - 1)
            for s in range(ring):
                step(steps - ring + s, s, None)
            relus_top(groups - 1)

        @block.tensor
        def _(pe):
            def bottom(g, column):
                for m in range(kb1):
                    last = pe.matmul(bot1_ps[:, m, :], bw0_sb[:, m * P:(m + 1) * P], dense_sb[:, bass.ds(column, wide)],
                                     start=True, stop=True)
                last.then_inc(bot1_done, 1)
                pe.wait_ge(bot1_relu, g + 1)
                for m in range(kb2):
                    for k in range(kb1):
                        last = pe.matmul(bot2_ps[:, m, :], bw1_sb[:, k, m * P:(m + 1) * P], bh1[:, k, :],
                                         start=(k == 0), stop=(k == kb1 - 1))
                last.then_inc(bot2_done, 1)
                pe.wait_ge(bot2_relu, g + 1)
                for k in range(kb2):
                    last = pe.matmul(bot2_ps[0:dim, kb2, :], bw2_sb[:, k, :], bh2[:, k, :],
                                     start=(k == 0), stop=(k == kb2 - 1))
                last.then_inc(bot3_done, 1)

            def step(g, u, s):
                pe.wait_ge(gathered[s], 16 * tables * (g + 1))
                for k in range(pairs):
                    last = pe.matmul(sums_ps[s % 2][:, k, :],
                                     fetched[:, s, 2 * k:2 * k + 2, :].rearrange("p t d -> p (t d)"),
                                     lane_sum[:, :], start=True, stop=True)
                last.then_inc(summed, 1)
                if s == 0:
                    pe.wait_ge(x_ready, g + 1)
                else:
                    pe.wait_ge(z_copied_act, u)
                    pe.wait_ge(z_copied_dve, u)
                pe.wait_ge(even_copied, u + 1)
                pe.wait_ge(odd_copied, u + 1)
                for n in range(quads):
                    four = vec[0:dim, s, 4 * n:4 * n + 4, :]
                    last = pe.matmul(z_ps[:, n, :].rearrange("p (b j) -> p b j", b=4)[:, :, 0:4 * column_sets],
                                     four.rearrange("p b i -> p (b i)"), four[:, :, 0:4 * column_sets],
                                     start=True, stop=True)
                last.then_inc(z_done, 1)

            def top(g):
                pe.wait_ge(z_copied_act, ring * g + ring)
                pe.wait_ge(z_copied_dve, ring * g + ring)
                for m in range(kt1):
                    pe.matmul(top1_ps[:, m, :], tw0x_sb[:, m * P:(m + 1) * P],
                              vec[:, :, :, 0].rearrange("d s b -> d (s b)"), start=True, stop=False)
                    for c in range(column_sets):
                        last = pe.matmul(top1_ps[:, m, :], tw0z_sb[:, c, m * P:(m + 1) * P],
                                         z[:, c, :, :].rearrange("p s b -> p (s b)"),
                                         start=False, stop=(c == column_sets - 1))
                last.then_inc(top1_done, 1)
                pe.wait_ge(top1_relu, g + 1)
                for m in range(kt2):
                    for k in range(kt1):
                        last = pe.matmul(top2_ps[:, m, :], tw1_sb[:, k, m * P:(m + 1) * P], th1[:, k, :],
                                         start=(k == 0), stop=(k == kt1 - 1))
                last.then_inc(top2_done, 1)
                pe.wait_ge(top2_relu, g + 1)
                for k in range(kt2):
                    last = pe.matmul(top2_ps[0:1, kt2, :], tw2_sb[:, k, :], th2[:, k, :],
                                     start=(k == 0), stop=(k == kt2 - 1))
                last.then_inc(top3_done, 1)

            pe.wait_ge(bot_loaded, 16 * 7)
            pe.wait_ge(ones_set, 1)
            pe.wait_ge(top_loaded, 16 * 7)
            pe.wait_ge(sum_made, 4)
            pe.wait_ge(vec_set, 1)
            with pe.Fori(0, groups) as g:
                bottom(g, g * wide)
                for s in range(ring):
                    step(g, ring * g + s, s)
                top(g)


def kernel(r_dense_x, r_sparse_idx, L0_rec_emb_tables, L0_rec_bot_W0, L0_rec_bot_b0, L0_rec_bot_W1, L0_rec_bot_b1,
           L0_rec_bot_W2, L0_rec_bot_b2, L0_rec_top_W0, L0_rec_top_b0, L0_rec_top_W1, L0_rec_top_b1, L0_rec_top_W2,
           L0_rec_top_b2):
    import numpy as np
    import concourse.bacc as bacc
    from concourse.bass_utils import run_bass_kernel_spmd

    samples, tables, _ = r_sparse_idx.shape
    dim = L0_rec_emb_tables.shape[2]
    steps = samples // Q
    vectors = tables + 1

    def transposed(w):
        w = np.asarray(w)
        return w.T.reshape(w.shape[1] // P, P, w.shape[0]).transpose(1, 0, 2)

    def by_partition(b):
        return np.asarray(b).reshape(-1, P).T

    top_w0 = np.asarray(L0_rec_top_W0)
    top_w0z = np.zeros((P, -(-vectors // 4), top_w0.shape[0]), top_w0.dtype)
    i, j = np.tril_indices(vectors, k=-1)
    top_w0z[Q * (j % 4) + i, j // 4, :] = top_w0[:, dim:].T

    arrays = {
        "dense": np.asarray(r_dense_x).reshape(Q, steps, -1).transpose(2, 1, 0),
        "sparse_idx": np.asarray(r_sparse_idx),
        "emb": np.asarray(L0_rec_emb_tables),
        "bw0": np.asarray(L0_rec_bot_W0).T,
        "bb0": np.asarray(L0_rec_bot_b0),
        "bw1": transposed(L0_rec_bot_W1),
        "bb1": by_partition(L0_rec_bot_b1),
        "bw2": transposed(L0_rec_bot_W2),
        "bb2": np.asarray(L0_rec_bot_b2).reshape(-1, 1),
        "tw0x": top_w0[:, :dim].T,
        "tw0z": top_w0z,
        "tb0": np.asarray(L0_rec_top_b0),
        "tw1": transposed(L0_rec_top_W1),
        "tb1": by_partition(L0_rec_top_b1),
        "tw2": transposed(L0_rec_top_W2),
        "tb2": np.asarray(L0_rec_top_b2),
    }
    arrays = {f"in_{name}": np.ascontiguousarray(a) for name, a in arrays.items()}
    nc = bacc.Bacc("TRN2", target_bir_lowering=False, num_devices=1)
    args = [nc.dram_tensor(name, a.shape, mybir.dt.from_np(a.dtype), kind="ExternalInput").ap() for name, a in arrays.items()]
    out = nc.dram_tensor("out_y", (samples, 1), F32, kind="ExternalOutput").ap()
    dlrm_kernel(nc, *args, out)
    return run_bass_kernel_spmd(nc, [arrays], core_ids=[0]).results[0]["out_y"]
```

```python
from contextlib import ExitStack

import concourse.bass as bass
from concourse import mybir

F32 = mybir.dt.float32
BF16 = mybir.dt.bfloat16
I32 = mybir.dt.int32
ALU = mybir.AluOpType
ACT = mybir.ActivationFunctionType
AX = mybir.AxisListType

P = 128
Q = 32
ACT_SAMPLES, DVE_SAMPLES = (0, 1), (2, 3)


def dlrm_kernel(nc, dense, sparse_idx, emb, bw0, bb0, bw1, bb1, bw2, bb2, tw0x, tw0z, tb0, tw1, tb1, tw2, tb2, out):
    dense_in, groups, lanes = dense.shape
    samples, tables, lookups = sparse_idx.shape
    rows_per_table = emb.shape[1]
    dim = emb.shape[2]
    assert lanes == P and groups * lanes == samples
    vectors = tables + 1
    assert 2 * dim == P and vectors <= Q
    h1, h2 = bw0.shape[1], bw1.shape[2]
    t1, t2 = tw0x.shape[1], tw1.shape[2]
    kb1, kb2, kt1, kt2 = h1 // P, h2 // P, t1 // P, t2 // P
    assert kb1 == kt1 == 4 and kb2 == kt2 == 2
    column_sets = -(-vectors // 4)

    fetched_tables = tables - 1
    kept = tables - 1
    pairs = -(-fetched_tables // 2)
    assert fetched_tables == 2 * pairs - 1 and pairs == 13
    quads = [range(0, 4), range(4, 8), range(8, 12), range(12, 13)]
    ids_a, ids_b = 7, pairs - 7
    turns = 8
    fours = lanes // turns // 4

    chunk_rows = 125
    chunks = rows_per_table // chunk_rows
    assert chunk_rows * chunks == rows_per_table
    batch = 5
    batches = chunks // batch
    ring = 5
    early = ring
    assert batches == 4 * ring
    pieces = 4
    piece = chunks // pieces

    emb_rows = emb.rearrange("t r d -> (t r) d")
    kept_rows = emb[kept].rearrange("(p c) d -> p c d", c=chunks)
    idx_by_lane = sparse_idx.rearrange("(p g) t l -> p (g t l)", g=groups)
    per_group = tables * lookups

    with ExitStack() as ctx:
        def sb(name, shape, dt=F32):
            return ctx.enter_context(nc.sbuf_tensor(name, shape, dt))

        def ps(name, shape):
            return ctx.enter_context(nc.psum_tensor(name, shape, F32))

        def sem(name):
            return ctx.enter_context(nc.semaphore(name))

        raw_idx = sb("raw_idx", [P, groups * per_group], I32)
        row_ids = sb("row_ids", [P, tables, lookups], I32)
        base_int = sb("base_int", [P, tables, lookups], I32)
        table_base = sb("table_base", [P, tables, lookups])
        fetched = sb("fetched", [P, pairs, 2, lookups, dim])
        sums = sb("sums", [P, pairs, 2, dim])
        identity = sb("identity", [P, P])
        ones = sb("ones", [P, P])
        zeros = sb("zeros", [P, P], BF16)
        vec = sb("vec", [dim + 1, lanes, Q])
        z = sb("z", [P, column_sets, lanes])
        raw_piece = sb("raw_piece", [chunk_rows, 2, piece, dim])
        high_mid = sb("high_mid", [chunk_rows, chunks, 2 * dim], BF16)
        low = sb("low", [chunk_rows, chunks, dim], BF16)
        row_int = sb("row_int", [chunk_rows, chunks], I32)
        row_of = sb("row_of", [chunk_rows, chunks])
        onehot = sb("onehot", [chunk_rows, ring * batch, lookups * lanes], BF16)
        spread = sb("spread", [P, lookups, lanes])
        mid_sums = sb("mid_sums", [dim, lookups, lanes])
        part_sums = sb("part_sums", [dim, 3, lanes])
        high_mid_sum = sb("high_mid_sum", [dim, lanes])
        dense_sb = sb("dense_sb", [dense_in + 1, groups * lanes])
        bw0_sb = sb("bw0_sb", [dense_in + 1, h1])
        bw1_sb = sb("bw1_sb", [P, kb1, h2])
        bb1_sb = sb("bb1_sb", [P, kb2])
        bw2_sb = sb("bw2_sb", [P, kb2, dim])
        bb2_sb = sb("bb2_sb", [dim, 1])
        bh1 = sb("bh1", [P, kb1, lanes])
        bh2 = sb("bh2", [P, kb2, lanes])
        tw0x_sb = sb("tw0x_sb", [dim + 1, t1])
        tw0z_sb = sb("tw0z_sb", [P, column_sets, t1])
        tw1_sb = sb("tw1_sb", [P, kt1, t2])
        tb1_sb = sb("tb1_sb", [P, kt2])
        tw2_sb = sb("tw2_sb", [P, kt2, 1])
        tb2_sb = sb("tb2_sb", [1, 1])
        th1 = sb("th1", [P, kt1, lanes])
        th2 = sb("th2", [P, kt2, lanes])
        y = sb("y", [1, lanes, groups])

        pair_ps = ps("pair_ps", [P, 4, lanes])
        z_ps = [ps(f"z_ps{i}", [P, fours, P]) for i in range(2)]
        index_ps = ps("index_ps", [P, lookups, lanes])
        high_mid_ps = ps("high_mid_ps", [P, lookups, lanes])
        low_ps = ps("low_ps", [P, lookups, lanes])
        first_ps = ps("first_ps", [P, kt1, lanes])
        rest_ps = ps("rest_ps", [P, 4, lanes])

        idx_first = sem("idx_first")
        idx_rest = sem("idx_rest")
        bot_loaded = sem("bot_loaded")
        top_loaded = sem("top_loaded")
        base_made = sem("base_made")
        rows_made = sem("rows_made")
        identity_made = sem("identity_made")
        consts_set = sem("consts_set")
        ids_ready = sem("ids_ready")
        gathered = [sem(f"gathered{k}") for k in range(pairs)]
        reduced = sem("reduced")
        quad_done = sem("quad_done")
        quad_copied = sem("quad_copied")
        bot1_done = sem("bot1_done")
        bot1_relu = sem("bot1_relu")
        bot2_done = sem("bot2_done")
        bot2_relu = sem("bot2_relu")
        bot3_done = sem("bot3_done")
        x_ready = sem("x_ready")
        z_done = sem("z_done")
        z_copied_act = sem("z_copied_act")
        z_copied_dve = sem("z_copied_dve")
        top1_done = sem("top1_done")
        top1_relu = sem("top1_relu")
        top2_done = sem("top2_done")
        top2_relu = sem("top2_relu")
        top3_done = sem("top3_done")
        y_ready = sem("y_ready")
        piece_in = [sem(f"piece_in{i}") for i in range(2)]
        high_made = sem("high_made")
        rest_made = sem("rest_made")
        mid_made = sem("mid_made")
        low_made = sem("low_made")
        spread_made = sem("spread_made")
        index_done = sem("index_done")
        onehot_made = sem("onehot_made")
        onehot_used = sem("onehot_used")
        mid_copied = sem("mid_copied")
        parts_summed = sem("parts_summed")
        high_mid_added = sem("high_mid_added")
        kept_ready = sem("kept_ready")
        stored = sem("stored")

        block = ctx.enter_context(nc.Block())

        def z_from(turn, r, q):
            return z_ps[turn % 2][r * Q:(r + 1) * Q, :, r * Q + q:r * Q + 4 * column_sets:4].rearrange("p n j -> p j n")

        def z_to(turn, r, q):
            return z[q * Q:(q + 1) * Q, :, turn * 4 * fours + r:(turn + 1) * 4 * fours:4]

        @block.sync
        def _(sp):
            sp.dma_start(raw_idx[:, 0:per_group], idx_by_lane[:, 0:per_group]).then_inc(idx_first, 16)
            sp.dma_start(raw_idx[:, per_group:], idx_by_lane[:, per_group:]).then_inc(idx_rest, 16)
            for n in range(pieces):
                if n == 2:
                    sp.dma_start(tw0x_sb[0:dim, :], tw0x).then_inc(top_loaded, 16)
                    sp.dma_start(tw0x_sb[dim:dim + 1, :], tb0.rearrange("(a n) -> a n", a=1)).then_inc(top_loaded, 16)
                    sp.dma_start(tw0z_sb[:, :, :], tw0z).then_inc(top_loaded, 16)
                    sp.dma_start(tw1_sb[:, :, :], tw1).then_inc(top_loaded, 16)
                    sp.dma_start(tb1_sb[:, :], tb1).then_inc(top_loaded, 16)
                    sp.dma_start(tw2_sb[:, :, :], tw2).then_inc(top_loaded, 16)
                    sp.dma_start(tb2_sb[:, :], tb2.rearrange("(a n) -> a n", a=1)).then_inc(top_loaded, 16)
                if n >= 2:
                    sp.wait_ge(low_made, n - 1)
                sp.dma_start(raw_piece[:, n % 2, :, :], kept_rows[:, n * piece:(n + 1) * piece, :]).then_inc(piece_in[n % 2], 16)
            sp.wait_ge(y_ready, groups)
            sp.dma_start(out.rearrange("(a n) c -> a (n c)", a=1), y.rearrange("a p g -> a (p g)")).then_inc(stored, 16)
            sp.wait_ge(stored, 16)

        @block.gpsimd
        def _(pool):
            pool.iota(base_int[:, :, :], pattern=[[rows_per_table, tables], [0, lookups]], base=0,
                      channel_multiplier=0).then_inc(base_made, 1)
            pool.wait_ge(base_made, 1)
            pool.tensor_copy(table_base[:, :, :], base_int[:, :, :]).then_inc(base_made, 1)
            pool.iota(row_int[:, :], pattern=[[1, chunks]], base=0, channel_multiplier=chunks).then_inc(rows_made, 1)
            pool.wait_ge(rows_made, 1)
            pool.tensor_copy(row_of[:, :], row_int[:, :]).then_inc(rows_made, 1)
            pool.memset(identity[:, :], 0.0).then_inc(identity_made, 1)
            pool.wait_ge(identity_made, 1)
            pool.affine_select(out=identity[:, :], in_=identity[:, :], compare_op=ALU.not_equal, fill=1.0, base=0,
                               pattern=[[-1, P]], channel_multiplier=1).then_inc(identity_made, 1)
            pool.wait_ge(rows_made, 2)
            pool.wait_ge(identity_made, 2)

            def gather(pair_range, end=fetched_tables):
                for k in pair_range:
                    for t in range(2 * k, min(2 * k + 2, end)):
                        for l in range(lookups):
                            pool.indirect_dma_start(
                                out=fetched[:, k, t % 2, l, :], out_offset=None, in_=emb_rows,
                                in_offset=bass.IndirectOffsetOnAxis(ap=row_ids[:, t, l:l + 1], axis=0),
                            ).then_inc(gathered[k], 16)

            pool.wait_ge(ids_ready, 1)
            gather(range(0, ids_a))
            pool.wait_ge(ids_ready, 2)
            gather(range(ids_a, pairs), tables)
            due_a = pool.alloc_register("due_a")
            due_b = pool.alloc_register("due_b")
            pool.reg_mov(due_a, 3)
            with pool.Fori(1, groups):
                pool.wait_ge(ids_ready, due_a)
                pool.reg_add(due_b, due_a, 1)
                gather(range(0, ids_a))
                pool.wait_ge(ids_ready, due_b)
                pool.reg_add(due_a, due_b, 1)
                gather(range(ids_a, pairs))

        @block.scalar
        def _(act):
            act.dma_start(bw0_sb[1:dense_in + 1, :], bw0).then_inc(bot_loaded, 16)
            act.dma_start(bw0_sb[0:1, :], bb0.rearrange("(a n) -> a n", a=1)).then_inc(bot_loaded, 16)
            act.dma_start(dense_sb[1:dense_in + 1, :], dense.rearrange("k g p -> k (g p)")).then_inc(bot_loaded, 16)
            act.dma_start(bw1_sb[:, :, :], bw1).then_inc(bot_loaded, 16)
            act.dma_start(bb1_sb[:, :], bb1).then_inc(bot_loaded, 16)
            act.dma_start(bw2_sb[:, :, :], bw2).then_inc(bot_loaded, 16)
            act.dma_start(bb2_sb[:, :], bb2).then_inc(bot_loaded, 16)
            for n in range(pieces):
                part = slice(n * piece, (n + 1) * piece)
                act.wait_ge(piece_in[n % 2], 16 * (n // 2 + 1))
                act.activation(high_mid[:, part, 0:dim], raw_piece[:, n % 2, :, :], ACT.Copy).then_inc(high_made, 1)
                act.wait_ge(rest_made, n + 1)
                act.activation(high_mid[:, part, dim:2 * dim], raw_piece[:, n % 2, :, :], ACT.Copy).then_inc(mid_made, 1)

            def copy_mid(g):
                act.wait_ge(onehot_used, batches * g)
                act.activation(mid_sums[:, :, :], high_mid_ps[dim:P, :, :], ACT.Copy).then_inc(mid_copied, 1)

            def group(g, gathers, build):
                for n, quad in enumerate(quads):
                    first, count = 2 * quad[0] + 1, len(quad)
                    act.wait_ge(quad_done, len(quads) * g + (n + 1))
                    last = act.activation(vec[0:dim, :, first:first + 2 * count:2].rearrange("p b k -> p k b"),
                                          pair_ps[0:dim, 0:count, :], ACT.Copy)
                    if 2 * quad[-1] + 1 < gathers:
                        last = act.activation(vec[0:dim, :, first + 1:first + 2 * count:2].rearrange("p b k -> p k b"),
                                              pair_ps[dim:P, 0:count, :], ACT.Copy)
                    last.then_inc(quad_copied, 1)
                if build:
                    copy_mid(g + 1)
                for turn in range(turns):
                    act.wait_ge(z_done, turns * g + (turn + 1))
                    for r in ACT_SAMPLES:
                        for q in range(4):
                            last = act.activation(z_to(turn, r, q), z_from(turn, r, q), ACT.Copy)
                    last.then_inc(z_copied_act, 1)
                act.wait_ge(top3_done, g + 1)
                act.activation(y[0:1, :, bass.ds(g, 1)].rearrange("a b g -> a (b g)"), rest_ps[0:1, 3, :],
                               ACT.Sigmoid, bias=tb2_sb[0:1, 0:1]).then_inc(y_ready, 1)

            act.wait_ge(top_loaded, 16 * 7)
            group(0, tables, True)
            with act.Fori(1, groups - 1) as g:
                group(g, fetched_tables, True)
            group(groups - 1, fetched_tables, False)

        @block.vector
        def _(dve):
            def make_ids(column, half, end=fetched_tables):
                at = slice(0, 2 * ids_a) if half == 0 else slice(2 * ids_a, end)
                index = raw_idx[:, bass.ds(column, per_group)].rearrange("p (t l) -> p t l", l=lookups)
                dve.tensor_tensor(row_ids[:, at, :], index[:, at, :], table_base[:, at, :], ALU.add).then_inc(ids_ready, 1)

            def spread_indices(column):
                index = raw_idx[:, bass.ds(column, per_group)].rearrange("p (t l) -> p l t", l=lookups)[:, :, kept:kept + 1]
                dve.tensor_tensor(spread[:, :, :], index.to_broadcast([P, lookups, lanes]),
                                  identity[:, :].unsqueeze(1).to_broadcast([P, lookups, lanes]),
                                  ALU.mult).then_inc(spread_made, 1)

            def make_onehot(n):
                for k in range(batch):
                    c = n * batch + k
                    last = dve.tensor_scalar(onehot[:, n % ring * batch + k, :],
                                             index_ps[0:chunk_rows, :, :].rearrange("p l b -> p (l b)"),
                                             row_of[:, c:c + 1], None, ALU.is_equal)
                last.then_inc(onehot_made, 1)

            def reduce(g, k, gathers, next_column):
                tables_here = min(2, gathers - 2 * k)
                if k < pairs - 1:
                    dve.wait_ge(gathered[k], 16 * lookups * 2 * (g + 1))
                else:
                    dve.wait_ge(gathered[k], 16 * lookups * (g + 2))
                dve.tensor_reduce(sums[:, k, 0:tables_here, :],
                                  fetched[:, k, 0:tables_here, :, :].rearrange("p t l d -> p t d l"),
                                  AX.X, ALU.add).then_inc(reduced, 1)
                if next_column is not None and k == ids_a - 1:
                    make_ids(next_column, 0)
                if next_column is not None and k == pairs - 1:
                    make_ids(next_column, 1)

            def add_parts(g):
                dve.wait_ge(mid_copied, g)
                for n, rows in enumerate((high_mid_ps[0:dim, :, :], mid_sums[:, :, :], low_ps[0:dim, :, :])):
                    last = dve.tensor_reduce(part_sums[:, n, :], rows.rearrange("p l b -> p b l"), AX.X, ALU.add)
                last.then_inc(parts_summed, 1)
                dve.wait_ge(parts_summed, g)
                dve.tensor_tensor(high_mid_sum[:, :], part_sums[:, 0, :], part_sums[:, 1, :], ALU.add).then_inc(high_mid_added, 1)
                dve.wait_ge(high_mid_added, g)
                dve.tensor_tensor(vec[0:dim, :, 1 + kept], high_mid_sum[:, :], part_sums[:, 2, :], ALU.add).then_inc(kept_ready, 1)

            def relu(g, n):
                if n == "top1":
                    dve.wait_ge(top1_done, g + 1)
                    dve.tensor_scalar(th1[:, :, :], first_ps[:, :, :], 0.0, None, ALU.max).then_inc(top1_relu, 1)
                if n == "top2":
                    dve.wait_ge(top2_done, g + 1)
                    for m in range(kt2):
                        last = dve.tensor_scalar(th2[:, m, :], rest_ps[:, m, :], tb1_sb[:, m:m + 1], 0.0, ALU.add, ALU.max)
                    last.then_inc(top2_relu, 1)
                if n == "bot1":
                    dve.wait_ge(bot1_done, g + 1)
                    dve.tensor_scalar(bh1[:, :, :], first_ps[:, :, :], 0.0, None, ALU.max).then_inc(bot1_relu, 1)
                if n == "bot2":
                    dve.wait_ge(bot2_done, g + 1)
                    for m in range(kb2):
                        last = dve.tensor_scalar(bh2[:, m, :], rest_ps[:, m, :], bb1_sb[:, m:m + 1], 0.0, ALU.add, ALU.max)
                    last.then_inc(bot2_relu, 1)
                if n == "x":
                    dve.wait_ge(bot3_done, g + 1)
                    dve.tensor_scalar(vec[0:dim, :, 0], rest_ps[0:dim, 2, :], bb2_sb[:, 0:1], 0.0, ALU.add,
                                      ALU.max).then_inc(x_ready, 1)

            def group(g, gathers, build, prepare):
                next_column = (g + 1) * per_group if build else None

                def ahead(first, end):
                    for n in range(first, end) if prepare else ():
                        dve.wait_ge(onehot_used, batches * g + (batches + n - ring + 1))
                        make_onehot(n)

                for k in range(4):
                    reduce(g, k, gathers, next_column)
                for k in range(4, 12):
                    if build:
                        for n in range(early + 2 * (k - 4), min(early + 2 * (k - 4) + 2, batches)):
                            dve.wait_ge(onehot_used, batches * g + (n - ring + 1))
                            make_onehot(n)
                    reduce(g, k, gathers, next_column)
                if prepare:
                    spread_indices((g + 2) * per_group)
                reduce(g, pairs - 1, gathers, next_column)
                for turn in range(turns):
                    dve.wait_ge(z_done, turns * g + (turn + 1))
                    for r in DVE_SAMPLES:
                        for q in range(4):
                            last = dve.tensor_copy(z_to(turn, r, q), z_from(turn, r, q))
                    last.then_inc(z_copied_dve, 1)
                if build:
                    add_parts(g + 1)
                if prepare:
                    dve.wait_ge(index_done, g + 2)
                ahead(0, 2)
                relu(g, "top1")
                ahead(2, 3)
                relu(g, "top2")
                if build:
                    relu(g + 1, "bot1")
                ahead(3, 4)
                if build:
                    relu(g + 1, "bot2")
                ahead(4, early)
                if build:
                    relu(g + 1, "x")

            dve.wait_ge(base_made, 2)
            dve.wait_ge(idx_first, 16)
            make_ids(0, 0)
            make_ids(0, 1, tables)
            dve.memset(ones[:, :], 1.0)
            dve.memset(zeros[:, :], 0.0)
            dve.memset(dense_sb[0:1, :], 1.0)
            dve.memset(vec[0:dim, :, vectors:Q], 0.0)
            dve.memset(vec[dim:dim + 1, :, 0], 1.0).then_inc(consts_set, 1)
            dve.wait_ge(identity_made, 2)
            dve.wait_ge(idx_rest, 16)
            spread_indices(per_group)
            dve.wait_ge(bot_loaded, 16 * 7)
            relu(0, "bot1")
            relu(0, "bot2")
            relu(0, "x")
            for n in range(pieces):
                part = slice(n * piece, (n + 1) * piece)
                raw = raw_piece[:, n % 2, :, :]
                dve.wait_ge(high_made, n + 1)
                dve.tensor_tensor(raw, raw, high_mid[:, part, 0:dim], ALU.subtract).then_inc(rest_made, 1)
                dve.wait_ge(mid_made, n + 1)
                dve.tensor_tensor(low[:, part, :], raw, high_mid[:, part, dim:2 * dim], ALU.subtract).then_inc(low_made, 1)
            dve.wait_ge(rows_made, 2)
            dve.wait_ge(index_done, 1)
            for n in range(early):
                make_onehot(n)
            dve.wait_ge(top_loaded, 16 * 7)
            group(0, tables, True, True)
            with dve.Fori(1, groups - 2) as g:
                group(g, fetched_tables, True, True)
            group(groups - 2, fetched_tables, True, False)
            group(groups - 1, fetched_tables, False, False)

        @block.tensor
        def _(pe):
            def bottom(g, follows):
                for m in range(kb1):
                    last = pe.matmul(first_ps[:, m, :], bw0_sb[:, m * P:(m + 1) * P], dense_sb[:, bass.ds(g * lanes, lanes)],
                                     start=True, stop=True)
                last.then_inc(bot1_done, 1)
                pe.wait_ge(bot1_relu, g + 1)
                if follows:
                    pe.wait_ge(y_ready, g)
                for m in range(kb2):
                    for k in range(kb1):
                        last = pe.matmul(rest_ps[:, m, :], bw1_sb[:, k, m * P:(m + 1) * P], bh1[:, k, :],
                                         start=(k == 0), stop=(k == kb1 - 1))
                last.then_inc(bot2_done, 1)
                pe.wait_ge(bot2_relu, g + 1)
                for k in range(kb2):
                    last = pe.matmul(rest_ps[0:dim, 2, :], bw2_sb[:, k, :], bh2[:, k, :],
                                     start=(k == 0), stop=(k == kb2 - 1))
                last.then_inc(bot3_done, 1)

            def broadcast_indices(g):
                pe.wait_ge(spread_made, g)
                pe.matmul(index_ps[:, :, :].rearrange("p l b -> p (l b)"), ones[:, :],
                          spread[:, :, :].rearrange("p l b -> p (l b)"), start=True, stop=True).then_inc(index_done, 1)

            high_mid_out = high_mid_ps[:, :, :].rearrange("p l b -> p (l b)")
            low_out = low_ps[0:dim, :, :].rearrange("p l b -> p (l b)")
            both = ((high_mid, high_mid_out), (low, low_out))

            def add_batch(first_chunk, slot, opens, closes):
                for k in range(batch):
                    for weights, rows in both:
                        w = weights[:, bass.ds(first_chunk + k, 1), :].rearrange("p c d -> p (c d)")
                        last = pe.matmul(rows, w, onehot[:, slot * batch + k, :],
                                         start=(opens and k == 0), stop=(closes and k == batch - 1))
                last.then_inc(onehot_used, 1)

            def add_round(n, made, opens=False, closes=False):
                for slot in range(ring):
                    pe.wait_ge(onehot_made, made + (slot + 1))
                    add_batch((n * ring + slot) * batch, slot, opens and slot == 0, closes and slot == ring - 1)

            def transposes(g, n, gathers):
                if n > 0:
                    pe.wait_ge(quad_copied, len(quads) * g + n)
                for k in quads[n]:
                    pe.wait_ge(reduced, pairs * g + (k + 1))
                    width = P if 2 * k + 1 < gathers else dim
                    last = pe.matmul(pair_ps[0:width, k - quads[n][0], :],
                                     sums[:, k, 0:width // dim, :].rearrange("p t d -> p (t d)"),
                                     identity[:, :], start=True, stop=True)
                last.then_inc(quad_done, 1)

            def gram(g, gathers):
                pe.wait_ge(x_ready, g + 1)
                if gathers < tables:
                    pe.wait_ge(kept_ready, g)
                pe.wait_ge(quad_copied, len(quads) * (g + 1))
                for turn in range(turns):
                    if turn >= 2:
                        pe.wait_ge(z_copied_act, turns * g + (turn - 1))
                        pe.wait_ge(z_copied_dve, turns * g + (turn - 1))
                    for n in range(fours):
                        b = 4 * (turn * fours + n)
                        four = vec[0:dim, b:b + 4, :]
                        last = pe.matmul(z_ps[turn % 2][:, n, :].rearrange("p (b j) -> p b j", b=4)[:, :, 0:4 * column_sets],
                                         four.rearrange("p b i -> p (b i)"), four[:, :, 0:4 * column_sets],
                                         start=True, stop=True)
                    last.then_inc(z_done, 1)

            def top(g):
                pe.wait_ge(z_copied_act, turns * (g + 1))
                pe.wait_ge(z_copied_dve, turns * (g + 1))
                for m in range(kt1):
                    pe.matmul(first_ps[:, m, :], tw0x_sb[:, m * P:(m + 1) * P], vec[:, :, 0], start=True, stop=False)
                    for c in range(column_sets):
                        last = pe.matmul(first_ps[:, m, :], tw0z_sb[:, c, m * P:(m + 1) * P], z[:, c, :],
                                         start=False, stop=(c == column_sets - 1))
                last.then_inc(top1_done, 1)
                pe.wait_ge(top1_relu, g + 1)
                for m in range(kt2):
                    for k in range(kt1):
                        last = pe.matmul(rest_ps[:, m, :], tw1_sb[:, k, m * P:(m + 1) * P], th1[:, k, :],
                                         start=(k == 0), stop=(k == kt1 - 1))
                last.then_inc(top2_done, 1)
                pe.wait_ge(top2_relu, g + 1)
                for k in range(kt2):
                    last = pe.matmul(rest_ps[0:1, 3, :], tw2_sb[:, k, :], th2[:, k, :],
                                     start=(k == 0), stop=(k == kt2 - 1))
                last.then_inc(top3_done, 1)

            def group(g, gathers, build, prepare):
                transposes(g, 0, gathers)
                if build:
                    if gathers < tables:
                        pe.wait_ge(kept_ready, g)
                    add_round(0, batches * g, opens=True)
                    add_round(1, batches * g + ring)
                transposes(g, 1, gathers)
                if build:
                    add_round(2, batches * g + 2 * ring)
                    add_round(3, batches * g + 3 * ring, closes=True)
                transposes(g, 2, gathers)
                transposes(g, 3, gathers)
                if prepare:
                    broadcast_indices(g + 2)
                gram(g, gathers)
                top(g)
                if build:
                    bottom(g + 1, True)

            pe.wait_ge(bot_loaded, 16 * 7)
            pe.wait_ge(consts_set, 1)
            bottom(0, False)
            broadcast_indices(1)
            pe.wait_ge(low_made, pieces)
            pe.wait_ge(mid_made, pieces)
            pe.wait_ge(identity_made, 2)
            pe.wait_ge(top_loaded, 16 * 7)
            group(0, tables, True, True)
            with pe.Fori(1, groups - 2) as g:
                group(g, fetched_tables, True, True)
            group(groups - 2, fetched_tables, True, False)
            group(groups - 1, fetched_tables, False, False)


def kernel(r_dense_x, r_sparse_idx, L0_rec_emb_tables, L0_rec_bot_W0, L0_rec_bot_b0, L0_rec_bot_W1, L0_rec_bot_b1,
           L0_rec_bot_W2, L0_rec_bot_b2, L0_rec_top_W0, L0_rec_top_b0, L0_rec_top_W1, L0_rec_top_b1, L0_rec_top_W2,
           L0_rec_top_b2):
    import numpy as np
    import concourse.bacc as bacc
    from concourse.bass_utils import run_bass_kernel_spmd

    samples, tables, _ = r_sparse_idx.shape
    dim = L0_rec_emb_tables.shape[2]
    groups = samples // P
    vectors = tables + 1

    def transposed(w):
        w = np.asarray(w)
        return w.T.reshape(w.shape[1] // P, P, w.shape[0]).transpose(1, 0, 2)

    def by_partition(b):
        return np.asarray(b).reshape(-1, P).T

    top_w0 = np.asarray(L0_rec_top_W0)
    top_w0z = np.zeros((P, -(-vectors // 4), top_w0.shape[0]), top_w0.dtype)
    i, j = np.tril_indices(vectors, k=-1)
    top_w0z[Q * (j % 4) + i, j // 4, :] = top_w0[:, dim:].T

    arrays = {
        "dense": np.asarray(r_dense_x).reshape(P, groups, -1).transpose(2, 1, 0),
        "sparse_idx": np.asarray(r_sparse_idx),
        "emb": np.asarray(L0_rec_emb_tables),
        "bw0": np.asarray(L0_rec_bot_W0).T,
        "bb0": np.asarray(L0_rec_bot_b0),
        "bw1": transposed(L0_rec_bot_W1),
        "bb1": by_partition(L0_rec_bot_b1),
        "bw2": transposed(L0_rec_bot_W2),
        "bb2": np.asarray(L0_rec_bot_b2).reshape(-1, 1),
        "tw0x": top_w0[:, :dim].T,
        "tw0z": top_w0z,
        "tb0": np.asarray(L0_rec_top_b0),
        "tw1": transposed(L0_rec_top_W1),
        "tb1": by_partition(L0_rec_top_b1),
        "tw2": transposed(L0_rec_top_W2),
        "tb2": np.asarray(L0_rec_top_b2),
    }
    arrays = {f"in_{name}": np.ascontiguousarray(a) for name, a in arrays.items()}
    nc = bacc.Bacc("TRN2", target_bir_lowering=False, num_devices=1)
    args = [nc.dram_tensor(name, a.shape, mybir.dt.from_np(a.dtype), kind="ExternalInput").ap() for name, a in arrays.items()]
    out = nc.dram_tensor("out_y", (samples, 1), F32, kind="ExternalOutput").ap()
    dlrm_kernel(nc, *args, out)
    return run_bass_kernel_spmd(nc, [arrays], core_ids=[0]).results[0]["out_y"]
```

```python
from contextlib import ExitStack

import concourse.bass as bass
from concourse import mybir

F32 = mybir.dt.float32
BF16 = mybir.dt.bfloat16
I32 = mybir.dt.int32
ALU = mybir.AluOpType
ACT = mybir.ActivationFunctionType
AX = mybir.AxisListType

P = 128
Q = 32
ACT_SAMPLES, DVE_SAMPLES = (0, 1), (2, 3)


def dlrm_kernel(nc, dense, sparse_idx, emb, bw0, bb0, bw1, bb1, bw2, bb2, tw0x, tw0z, tb0, tw1, tb1, tw2, tb2, out):
    dense_in, groups, lanes = dense.shape
    samples, tables, lookups = sparse_idx.shape
    rows_per_table = emb.shape[1]
    dim = emb.shape[2]
    assert lanes == P and groups * lanes == samples
    vectors = tables + 1
    assert 2 * dim == P and vectors <= Q
    h1, h2 = bw0.shape[1], bw1.shape[2]
    t1, t2 = tw0x.shape[1], tw1.shape[2]
    kb1, kb2, kt1, kt2 = h1 // P, h2 // P, t1 // P, t2 // P
    assert kb1 == kt1 == 4 and kb2 == kt2 == 2
    column_sets = -(-vectors // 4)
    all_sets = range(column_sets)
    first_sets, last_sets = range(0, 4), range(4, column_sets)

    fetched_tables = tables - 1
    kept = tables - 1
    pairs = -(-fetched_tables // 2)
    assert fetched_tables == 2 * pairs - 1 and pairs == 13
    quads = [range(0, 4), range(4, 8), range(8, 12), range(12, 13)]
    ids_a, ids_b = 7, pairs - 7
    turns = 8
    fours = lanes // turns // 4

    chunk_rows = 125
    chunks = rows_per_table // chunk_rows
    assert chunk_rows * chunks == rows_per_table
    batch = 5
    batches = chunks // batch
    ring = 5
    early = ring
    assert batches == 4 * ring
    pieces = 4
    piece = chunks // pieces

    emb_rows = emb.rearrange("t r d -> (t r) d")
    kept_rows = emb[kept].rearrange("(p c) d -> p c d", c=chunks)
    idx_by_lane = sparse_idx.rearrange("(p g) t l -> p (g t l)", g=groups)
    per_group = tables * lookups

    with ExitStack() as ctx:
        def sb(name, shape, dt=F32):
            return ctx.enter_context(nc.sbuf_tensor(name, shape, dt))

        def ps(name, shape):
            return ctx.enter_context(nc.psum_tensor(name, shape, F32))

        def sem(name):
            return ctx.enter_context(nc.semaphore(name))

        raw_idx = sb("raw_idx", [P, groups * per_group], I32)
        row_ids = sb("row_ids", [P, tables, lookups], I32)
        base_int = sb("base_int", [P, tables, lookups], I32)
        table_base = sb("table_base", [P, tables, lookups])
        fetched = sb("fetched", [P, pairs, 2, lookups, dim])
        sums = sb("sums", [P, pairs, 2, dim])
        identity = sb("identity", [P, P])
        ones = sb("ones", [P, P])
        zeros = sb("zeros", [P, P], BF16)
        vec = sb("vec", [dim + 1, lanes, Q])
        z = sb("z", [P, column_sets, lanes])
        raw_piece = sb("raw_piece", [chunk_rows, 2, piece, dim])
        high_mid = sb("high_mid", [chunk_rows, chunks, 2 * dim], BF16)
        low = sb("low", [chunk_rows, chunks, dim], BF16)
        row_int = sb("row_int", [chunk_rows, chunks], I32)
        row_of = sb("row_of", [chunk_rows, chunks])
        onehot = sb("onehot", [chunk_rows, ring * batch, lookups * lanes], BF16)
        spread = sb("spread", [P, lookups, lanes])
        mid_sums = sb("mid_sums", [dim, lookups, lanes])
        part_sums = sb("part_sums", [dim, 3, lanes])
        high_mid_sum = sb("high_mid_sum", [dim, lanes])
        dense_sb = sb("dense_sb", [dense_in + 1, groups * lanes])
        bw0_sb = sb("bw0_sb", [dense_in + 1, h1])
        bw1_sb = sb("bw1_sb", [P, kb1, h2])
        bb1_sb = sb("bb1_sb", [P, kb2])
        bw2_sb = sb("bw2_sb", [P, kb2, dim])
        bb2_sb = sb("bb2_sb", [dim, 1])
        bh1 = sb("bh1", [P, kb1, lanes])
        bh2 = sb("bh2", [P, kb2, lanes])
        tw0x_sb = sb("tw0x_sb", [dim + 1, t1])
        tw0z_sb = sb("tw0z_sb", [P, column_sets, t1])
        tw1_sb = sb("tw1_sb", [P, kt1, t2])
        tb1_sb = sb("tb1_sb", [P, kt2])
        tw2_sb = sb("tw2_sb", [P, kt2, 1])
        tb2_sb = sb("tb2_sb", [1, 1])
        th1 = sb("th1", [P, kt1, lanes])
        th2 = sb("th2", [P, kt2, lanes])
        y = sb("y", [1, lanes, groups])

        pair_ps = ps("pair_ps", [P, 4, lanes])
        z_ps = [ps(f"z_ps{i}", [P, fours, P]) for i in range(2)]
        index_ps = ps("index_ps", [P, lookups, lanes])
        high_mid_ps = ps("high_mid_ps", [P, lookups, lanes])
        low_ps = ps("low_ps", [P, lookups, lanes])
        first_ps = ps("first_ps", [P, kt1, lanes])
        rest_ps = ps("rest_ps", [P, 4, lanes])

        idx_first = sem("idx_first")
        idx_rest = sem("idx_rest")
        bot_loaded = sem("bot_loaded")
        top_loaded = sem("top_loaded")
        base_made = sem("base_made")
        rows_made = sem("rows_made")
        identity_made = sem("identity_made")
        consts_set = sem("consts_set")
        ids_ready = sem("ids_ready")
        gathered = [sem(f"gathered{k}") for k in range(pairs)]
        reduced = sem("reduced")
        quad_done = sem("quad_done")
        quad_copied = sem("quad_copied")
        bot1_done = sem("bot1_done")
        bot1_relu = sem("bot1_relu")
        bot2_done = sem("bot2_done")
        bot2_relu = sem("bot2_relu")
        bot3_done = sem("bot3_done")
        x_ready = sem("x_ready")
        z_done = sem("z_done")
        z_copied_act = sem("z_copied_act")
        z_copied_dve = sem("z_copied_dve")
        top1_done = sem("top1_done")
        top1_relu = sem("top1_relu")
        top2_done = sem("top2_done")
        top2_relu = sem("top2_relu")
        top3_done = sem("top3_done")
        y_ready = sem("y_ready")
        piece_in = [sem(f"piece_in{i}") for i in range(2)]
        high_made = sem("high_made")
        rest_made = sem("rest_made")
        mid_made = sem("mid_made")
        low_made = sem("low_made")
        spread_made = sem("spread_made")
        index_done = sem("index_done")
        onehot_made = sem("onehot_made")
        onehot_used = sem("onehot_used")
        mid_copied = sem("mid_copied")
        parts_summed = sem("parts_summed")
        high_mid_added = sem("high_mid_added")
        kept_ready = sem("kept_ready")
        stored = sem("stored")

        block = ctx.enter_context(nc.Block())

        def z_from(turn, r, q, sets):
            columns = slice(r * Q + 4 * sets[0] + q, r * Q + 4 * sets[-1] + 4, 4)
            return z_ps[turn % 2][r * Q:(r + 1) * Q, :, columns].rearrange("p n j -> p j n")

        def z_to(turn, r, q, sets):
            return z[q * Q:(q + 1) * Q, sets[0]:sets[-1] + 1, turn * 4 * fours + r:(turn + 1) * 4 * fours:4]

        @block.sync
        def _(sp):
            sp.dma_start(raw_idx[:, 0:per_group], idx_by_lane[:, 0:per_group]).then_inc(idx_first, 16)
            sp.dma_start(raw_idx[:, per_group:], idx_by_lane[:, per_group:]).then_inc(idx_rest, 16)
            for n in range(pieces):
                if n == 2:
                    sp.dma_start(tw0x_sb[0:dim, :], tw0x).then_inc(top_loaded, 16)
                    sp.dma_start(tw0x_sb[dim:dim + 1, :], tb0.rearrange("(a n) -> a n", a=1)).then_inc(top_loaded, 16)
                    sp.dma_start(tw0z_sb[:, :, :], tw0z).then_inc(top_loaded, 16)
                    sp.dma_start(tw1_sb[:, :, :], tw1).then_inc(top_loaded, 16)
                    sp.dma_start(tb1_sb[:, :], tb1).then_inc(top_loaded, 16)
                    sp.dma_start(tw2_sb[:, :, :], tw2).then_inc(top_loaded, 16)
                    sp.dma_start(tb2_sb[:, :], tb2.rearrange("(a n) -> a n", a=1)).then_inc(top_loaded, 16)
                if n >= 2:
                    sp.wait_ge(low_made, n - 1)
                sp.dma_start(raw_piece[:, n % 2, :, :], kept_rows[:, n * piece:(n + 1) * piece, :]).then_inc(piece_in[n % 2], 16)
            sp.wait_ge(y_ready, groups)
            sp.dma_start(out.rearrange("(a n) c -> a (n c)", a=1), y.rearrange("a p g -> a (p g)")).then_inc(stored, 16)
            sp.wait_ge(stored, 16)

        @block.gpsimd
        def _(pool):
            pool.iota(base_int[:, :, :], pattern=[[rows_per_table, tables], [0, lookups]], base=0,
                      channel_multiplier=0).then_inc(base_made, 1)
            pool.wait_ge(base_made, 1)
            pool.tensor_copy(table_base[:, :, :], base_int[:, :, :]).then_inc(base_made, 1)
            pool.iota(row_int[:, :], pattern=[[1, chunks]], base=0, channel_multiplier=chunks).then_inc(rows_made, 1)
            pool.wait_ge(rows_made, 1)
            pool.tensor_copy(row_of[:, :], row_int[:, :]).then_inc(rows_made, 1)
            pool.memset(identity[:, :], 0.0).then_inc(identity_made, 1)
            pool.wait_ge(identity_made, 1)
            pool.affine_select(out=identity[:, :], in_=identity[:, :], compare_op=ALU.not_equal, fill=1.0, base=0,
                               pattern=[[-1, P]], channel_multiplier=1).then_inc(identity_made, 1)
            pool.wait_ge(rows_made, 2)
            pool.wait_ge(identity_made, 2)

            def gather(pair_range, end=fetched_tables):
                for k in pair_range:
                    for t in range(2 * k, min(2 * k + 2, end)):
                        for l in range(lookups):
                            pool.indirect_dma_start(
                                out=fetched[:, k, t % 2, l, :], out_offset=None, in_=emb_rows,
                                in_offset=bass.IndirectOffsetOnAxis(ap=row_ids[:, t, l:l + 1], axis=0),
                            ).then_inc(gathered[k], 16)

            pool.wait_ge(ids_ready, 1)
            gather(range(0, ids_a))
            pool.wait_ge(ids_ready, 2)
            gather(range(ids_a, pairs), tables)
            due_a = pool.alloc_register("due_a")
            due_b = pool.alloc_register("due_b")
            pool.reg_mov(due_a, 3)
            with pool.Fori(1, groups):
                pool.wait_ge(ids_ready, due_a)
                pool.reg_add(due_b, due_a, 1)
                gather(range(0, ids_a))
                pool.wait_ge(ids_ready, due_b)
                pool.reg_add(due_a, due_b, 1)
                gather(range(ids_a, pairs))

        @block.scalar
        def _(act):
            act.dma_start(bw0_sb[1:dense_in + 1, :], bw0).then_inc(bot_loaded, 16)
            act.dma_start(bw0_sb[0:1, :], bb0.rearrange("(a n) -> a n", a=1)).then_inc(bot_loaded, 16)
            act.dma_start(dense_sb[1:dense_in + 1, :], dense.rearrange("k g p -> k (g p)")).then_inc(bot_loaded, 16)
            act.dma_start(bw1_sb[:, :, :], bw1).then_inc(bot_loaded, 16)
            act.dma_start(bb1_sb[:, :], bb1).then_inc(bot_loaded, 16)
            act.dma_start(bw2_sb[:, :, :], bw2).then_inc(bot_loaded, 16)
            act.dma_start(bb2_sb[:, :], bb2).then_inc(bot_loaded, 16)
            for n in range(pieces):
                part = slice(n * piece, (n + 1) * piece)
                act.wait_ge(piece_in[n % 2], 16 * (n // 2 + 1))
                act.activation(high_mid[:, part, 0:dim], raw_piece[:, n % 2, :, :], ACT.Copy).then_inc(high_made, 1)
                act.wait_ge(rest_made, n + 1)
                act.activation(high_mid[:, part, dim:2 * dim], raw_piece[:, n % 2, :, :], ACT.Copy).then_inc(mid_made, 1)

            def copy_mid(g):
                act.wait_ge(onehot_used, batches * g)
                act.activation(mid_sums[:, :, :], high_mid_ps[dim:P, :, :], ACT.Copy).then_inc(mid_copied, 1)

            def copy_quads(g, gathers, first_quad, end_quad):
                for n in range(first_quad, end_quad):
                    quad = quads[n]
                    first, count = 2 * quad[0] + 1, len(quad)
                    act.wait_ge(quad_done, len(quads) * g + (n + 1))
                    last = act.activation(vec[0:dim, :, first:first + 2 * count:2].rearrange("p b k -> p k b"),
                                          pair_ps[0:dim, 0:count, :], ACT.Copy)
                    if 2 * quad[-1] + 1 < gathers:
                        last = act.activation(vec[0:dim, :, first + 1:first + 2 * count:2].rearrange("p b k -> p k b"),
                                              pair_ps[dim:P, 0:count, :], ACT.Copy)
                    last.then_inc(quad_copied, 1)

            def copy_z(begun, sets):
                for turn in range(turns):
                    act.wait_ge(z_done, begun + (turn + 1))
                    for r in ACT_SAMPLES:
                        for q in range(4):
                            last = act.activation(z_to(turn, r, q, sets), z_from(turn, r, q, sets), ACT.Copy)
                    last.then_inc(z_copied_act, 1)

            def finish(g):
                act.wait_ge(top3_done, g + 1)
                act.activation(y[0:1, :, bass.ds(g, 1)].rearrange("a b g -> a (b g)"), rest_ps[0:1, 3, :],
                               ACT.Sigmoid, bias=tb2_sb[0:1, 0:1]).then_inc(y_ready, 1)

            def group(g, gathers):
                copy_quads(g, gathers, 0, len(quads))
                copy_mid(g + 1)
                copy_z(turns * g, all_sets)
                finish(g)

            def last_group(g):
                copy_quads(g, fetched_tables, 0, 2)
                copy_z(turns * g, first_sets)
                copy_quads(g, fetched_tables, 2, len(quads))
                copy_z(turns * (g + 1), last_sets)
                finish(g)

            act.wait_ge(top_loaded, 16 * 7)
            group(0, tables)
            with act.Fori(1, groups - 1) as g:
                group(g, fetched_tables)
            last_group(groups - 1)

        @block.vector
        def _(dve):
            def make_ids(column, half, end=fetched_tables):
                at = slice(0, 2 * ids_a) if half == 0 else slice(2 * ids_a, end)
                index = raw_idx[:, bass.ds(column, per_group)].rearrange("p (t l) -> p t l", l=lookups)
                dve.tensor_tensor(row_ids[:, at, :], index[:, at, :], table_base[:, at, :], ALU.add).then_inc(ids_ready, 1)

            def spread_indices(column):
                index = raw_idx[:, bass.ds(column, per_group)].rearrange("p (t l) -> p l t", l=lookups)[:, :, kept:kept + 1]
                dve.tensor_tensor(spread[:, :, :], index.to_broadcast([P, lookups, lanes]),
                                  identity[:, :].unsqueeze(1).to_broadcast([P, lookups, lanes]),
                                  ALU.mult).then_inc(spread_made, 1)

            def make_onehot(n):
                for k in range(batch):
                    c = n * batch + k
                    last = dve.tensor_scalar(onehot[:, n % ring * batch + k, :],
                                             index_ps[0:chunk_rows, :, :].rearrange("p l b -> p (l b)"),
                                             row_of[:, c:c + 1], None, ALU.is_equal)
                last.then_inc(onehot_made, 1)

            def reduce(g, k, gathers, next_column):
                tables_here = min(2, gathers - 2 * k)
                if k < pairs - 1:
                    dve.wait_ge(gathered[k], 16 * lookups * 2 * (g + 1))
                else:
                    dve.wait_ge(gathered[k], 16 * lookups * (g + 2))
                dve.tensor_reduce(sums[:, k, 0:tables_here, :],
                                  fetched[:, k, 0:tables_here, :, :].rearrange("p t l d -> p t d l"),
                                  AX.X, ALU.add).then_inc(reduced, 1)
                if next_column is not None and k == ids_a - 1:
                    make_ids(next_column, 0)
                if next_column is not None and k == pairs - 1:
                    make_ids(next_column, 1)

            def add_parts(g):
                dve.wait_ge(mid_copied, g)
                for n, rows in enumerate((high_mid_ps[0:dim, :, :], mid_sums[:, :, :], low_ps[0:dim, :, :])):
                    last = dve.tensor_reduce(part_sums[:, n, :], rows.rearrange("p l b -> p b l"), AX.X, ALU.add)
                last.then_inc(parts_summed, 1)
                dve.wait_ge(parts_summed, g)
                dve.tensor_tensor(high_mid_sum[:, :], part_sums[:, 0, :], part_sums[:, 1, :], ALU.add).then_inc(high_mid_added, 1)
                dve.wait_ge(high_mid_added, g)
                dve.tensor_tensor(vec[0:dim, :, 1 + kept], high_mid_sum[:, :], part_sums[:, 2, :], ALU.add).then_inc(kept_ready, 1)

            def relu(g, n):
                if n == "top1":
                    dve.wait_ge(top1_done, g + 1)
                    dve.tensor_scalar(th1[:, :, :], first_ps[:, :, :], 0.0, None, ALU.max).then_inc(top1_relu, 1)
                if n == "top2":
                    dve.wait_ge(top2_done, g + 1)
                    for m in range(kt2):
                        last = dve.tensor_scalar(th2[:, m, :], rest_ps[:, m, :], tb1_sb[:, m:m + 1], 0.0, ALU.add, ALU.max)
                    last.then_inc(top2_relu, 1)
                if n == "bot1":
                    dve.wait_ge(bot1_done, g + 1)
                    dve.tensor_scalar(bh1[:, :, :], first_ps[:, :, :], 0.0, None, ALU.max).then_inc(bot1_relu, 1)
                if n == "bot2":
                    dve.wait_ge(bot2_done, g + 1)
                    for m in range(kb2):
                        last = dve.tensor_scalar(bh2[:, m, :], rest_ps[:, m, :], bb1_sb[:, m:m + 1], 0.0, ALU.add, ALU.max)
                    last.then_inc(bot2_relu, 1)
                if n == "x":
                    dve.wait_ge(bot3_done, g + 1)
                    dve.tensor_scalar(vec[0:dim, :, 0], rest_ps[0:dim, 2, :], bb2_sb[:, 0:1], 0.0, ALU.add,
                                      ALU.max).then_inc(x_ready, 1)

            def copy_z(begun, sets):
                for turn in range(turns):
                    dve.wait_ge(z_done, begun + (turn + 1))
                    for r in DVE_SAMPLES:
                        for q in range(4):
                            last = dve.tensor_copy(z_to(turn, r, q, sets), z_from(turn, r, q, sets))
                    last.then_inc(z_copied_dve, 1)

            def group(g, gathers, prepare):
                next_column = (g + 1) * per_group

                def ahead(first, end):
                    for n in range(first, end) if prepare else ():
                        dve.wait_ge(onehot_used, batches * g + (batches + n - ring + 1))
                        make_onehot(n)

                for k in range(4):
                    reduce(g, k, gathers, next_column)
                for k in range(4, 12):
                    for n in range(early + 2 * (k - 4), min(early + 2 * (k - 4) + 2, batches)):
                        dve.wait_ge(onehot_used, batches * g + (n - ring + 1))
                        make_onehot(n)
                    reduce(g, k, gathers, next_column)
                if prepare:
                    spread_indices((g + 2) * per_group)
                reduce(g, pairs - 1, gathers, next_column)
                copy_z(turns * g, all_sets)
                add_parts(g + 1)
                if prepare:
                    dve.wait_ge(index_done, g + 2)
                ahead(0, 2)
                relu(g, "top1")
                ahead(2, 3)
                relu(g, "top2")
                relu(g + 1, "bot1")
                ahead(3, 4)
                relu(g + 1, "bot2")
                ahead(4, early)
                relu(g + 1, "x")

            def last_group(g):
                for k in range(0, 8):
                    reduce(g, k, fetched_tables, None)
                copy_z(turns * g, first_sets)
                for k in range(8, pairs):
                    reduce(g, k, fetched_tables, None)
                copy_z(turns * (g + 1), last_sets)
                relu(g, "top1")
                relu(g, "top2")

            dve.wait_ge(base_made, 2)
            dve.wait_ge(idx_first, 16)
            make_ids(0, 0)
            make_ids(0, 1, tables)
            dve.memset(ones[:, :], 1.0)
            dve.memset(zeros[:, :], 0.0)
            dve.memset(dense_sb[0:1, :], 1.0)
            dve.memset(vec[0:dim, :, vectors:Q], 0.0)
            dve.memset(vec[dim:dim + 1, :, 0], 1.0).then_inc(consts_set, 1)
            dve.wait_ge(identity_made, 2)
            dve.wait_ge(idx_rest, 16)
            spread_indices(per_group)
            dve.wait_ge(bot_loaded, 16 * 7)
            relu(0, "bot1")
            relu(0, "bot2")
            relu(0, "x")
            for n in range(pieces):
                part = slice(n * piece, (n + 1) * piece)
                raw = raw_piece[:, n % 2, :, :]
                dve.wait_ge(high_made, n + 1)
                dve.tensor_tensor(raw, raw, high_mid[:, part, 0:dim], ALU.subtract).then_inc(rest_made, 1)
                dve.wait_ge(mid_made, n + 1)
                dve.tensor_tensor(low[:, part, :], raw, high_mid[:, part, dim:2 * dim], ALU.subtract).then_inc(low_made, 1)
            dve.wait_ge(rows_made, 2)
            dve.wait_ge(index_done, 1)
            for n in range(early):
                make_onehot(n)
            dve.wait_ge(top_loaded, 16 * 7)
            group(0, tables, True)
            with dve.Fori(1, groups - 2) as g:
                group(g, fetched_tables, True)
            group(groups - 2, fetched_tables, False)
            last_group(groups - 1)

        @block.tensor
        def _(pe):
            def bottom(g, follows):
                for m in range(kb1):
                    last = pe.matmul(first_ps[:, m, :], bw0_sb[:, m * P:(m + 1) * P], dense_sb[:, bass.ds(g * lanes, lanes)],
                                     start=True, stop=True)
                last.then_inc(bot1_done, 1)
                pe.wait_ge(bot1_relu, g + 1)
                if follows:
                    pe.wait_ge(y_ready, g)
                for m in range(kb2):
                    for k in range(kb1):
                        last = pe.matmul(rest_ps[:, m, :], bw1_sb[:, k, m * P:(m + 1) * P], bh1[:, k, :],
                                         start=(k == 0), stop=(k == kb1 - 1))
                last.then_inc(bot2_done, 1)
                pe.wait_ge(bot2_relu, g + 1)
                for k in range(kb2):
                    last = pe.matmul(rest_ps[0:dim, 2, :], bw2_sb[:, k, :], bh2[:, k, :],
                                     start=(k == 0), stop=(k == kb2 - 1))
                last.then_inc(bot3_done, 1)

            def broadcast_indices(g):
                pe.wait_ge(spread_made, g)
                pe.matmul(index_ps[:, :, :].rearrange("p l b -> p (l b)"), ones[:, :],
                          spread[:, :, :].rearrange("p l b -> p (l b)"), start=True, stop=True).then_inc(index_done, 1)

            high_mid_out = high_mid_ps[:, :, :].rearrange("p l b -> p (l b)")
            low_out = low_ps[0:dim, :, :].rearrange("p l b -> p (l b)")
            both = ((high_mid, high_mid_out), (low, low_out))

            def add_batch(first_chunk, slot, opens, closes):
                for k in range(batch):
                    for weights, rows in both:
                        w = weights[:, bass.ds(first_chunk + k, 1), :].rearrange("p c d -> p (c d)")
                        last = pe.matmul(rows, w, onehot[:, slot * batch + k, :],
                                         start=(opens and k == 0), stop=(closes and k == batch - 1))
                last.then_inc(onehot_used, 1)

            def add_round(n, made, opens=False, closes=False):
                for slot in range(ring):
                    pe.wait_ge(onehot_made, made + (slot + 1))
                    add_batch((n * ring + slot) * batch, slot, opens and slot == 0, closes and slot == ring - 1)

            def transposes(g, n, gathers):
                if n > 0:
                    pe.wait_ge(quad_copied, len(quads) * g + n)
                for k in quads[n]:
                    pe.wait_ge(reduced, pairs * g + (k + 1))
                    width = P if 2 * k + 1 < gathers else dim
                    last = pe.matmul(pair_ps[0:width, k - quads[n][0], :],
                                     sums[:, k, 0:width // dim, :].rearrange("p t d -> p (t d)"),
                                     identity[:, :], start=True, stop=True)
                last.then_inc(quad_done, 1)

            def gram(begun, sets):
                for turn in range(turns):
                    if turn >= 2:
                        pe.wait_ge(z_copied_act, begun + (turn - 1))
                        pe.wait_ge(z_copied_dve, begun + (turn - 1))
                    columns = slice(4 * sets[0], 4 * sets[-1] + 4)
                    for n in range(fours):
                        b = 4 * (turn * fours + n)
                        four = vec[0:dim, b:b + 4, :]
                        last = pe.matmul(z_ps[turn % 2][:, n, :].rearrange("p (b j) -> p b j", b=4)[:, :, columns],
                                         four.rearrange("p b i -> p (b i)"), four[:, :, columns],
                                         start=True, stop=True)
                    last.then_inc(z_done, 1)

            def top_first(begun, sets):
                pe.wait_ge(z_copied_act, begun + turns)
                pe.wait_ge(z_copied_dve, begun + turns)
                for m in range(kt1):
                    if sets[0] == 0:
                        pe.matmul(first_ps[:, m, :], tw0x_sb[:, m * P:(m + 1) * P], vec[:, :, 0],
                                  start=(m == 0), stop=False, skip_group_check=True)
                    for c in sets:
                        last = pe.matmul(first_ps[:, m, :], tw0z_sb[:, c, m * P:(m + 1) * P], z[:, c, :],
                                         start=False, stop=(c == column_sets - 1), skip_group_check=True)
                return last

            def top_rest(g):
                pe.wait_ge(top1_relu, g + 1)
                for m in range(kt2):
                    for k in range(kt1):
                        last = pe.matmul(rest_ps[:, m, :], tw1_sb[:, k, m * P:(m + 1) * P], th1[:, k, :],
                                         start=(k == 0), stop=(k == kt1 - 1))
                last.then_inc(top2_done, 1)
                pe.wait_ge(top2_relu, g + 1)
                for k in range(kt2):
                    last = pe.matmul(rest_ps[0:1, 3, :], tw2_sb[:, k, :], th2[:, k, :],
                                     start=(k == 0), stop=(k == kt2 - 1))
                last.then_inc(top3_done, 1)

            def group(g, gathers, prepare):
                transposes(g, 0, gathers)
                if gathers < tables:
                    pe.wait_ge(kept_ready, g)
                add_round(0, batches * g, opens=True)
                add_round(1, batches * g + ring)
                transposes(g, 1, gathers)
                add_round(2, batches * g + 2 * ring)
                add_round(3, batches * g + 3 * ring, closes=True)
                transposes(g, 2, gathers)
                transposes(g, 3, gathers)
                if prepare:
                    broadcast_indices(g + 2)
                pe.wait_ge(x_ready, g + 1)
                pe.wait_ge(quad_copied, len(quads) * g + len(quads))
                gram(turns * g, all_sets)
                top_first(turns * g, all_sets).then_inc(top1_done, 1)
                top_rest(g)
                bottom(g + 1, True)

            def last_group(g):
                transposes(g, 0, fetched_tables)
                transposes(g, 1, fetched_tables)
                pe.wait_ge(x_ready, g + 1)
                pe.wait_ge(kept_ready, g)
                pe.wait_ge(quad_copied, len(quads) * g + 2)
                gram(turns * g, first_sets)
                top_first(turns * g, first_sets)
                transposes(g, 2, fetched_tables)
                transposes(g, 3, fetched_tables)
                pe.wait_ge(quad_copied, len(quads) * (g + 1))
                gram(turns * (g + 1), last_sets)
                top_first(turns * (g + 1), last_sets).then_inc(top1_done, 1)
                top_rest(g)

            pe.wait_ge(bot_loaded, 16 * 7)
            pe.wait_ge(consts_set, 1)
            bottom(0, False)
            broadcast_indices(1)
            pe.wait_ge(low_made, pieces)
            pe.wait_ge(mid_made, pieces)
            pe.wait_ge(identity_made, 2)
            pe.wait_ge(top_loaded, 16 * 7)
            group(0, tables, True)
            with pe.Fori(1, groups - 2) as g:
                group(g, fetched_tables, True)
            group(groups - 2, fetched_tables, False)
            last_group(groups - 1)


def kernel(r_dense_x, r_sparse_idx, L0_rec_emb_tables, L0_rec_bot_W0, L0_rec_bot_b0, L0_rec_bot_W1, L0_rec_bot_b1,
           L0_rec_bot_W2, L0_rec_bot_b2, L0_rec_top_W0, L0_rec_top_b0, L0_rec_top_W1, L0_rec_top_b1, L0_rec_top_W2,
           L0_rec_top_b2):
    import numpy as np
    import concourse.bacc as bacc
    from concourse.bass_utils import run_bass_kernel_spmd

    samples, tables, _ = r_sparse_idx.shape
    dim = L0_rec_emb_tables.shape[2]
    groups = samples // P
    vectors = tables + 1

    def transposed(w):
        w = np.asarray(w)
        return w.T.reshape(w.shape[1] // P, P, w.shape[0]).transpose(1, 0, 2)

    def by_partition(b):
        return np.asarray(b).reshape(-1, P).T

    top_w0 = np.asarray(L0_rec_top_W0)
    top_w0z = np.zeros((P, -(-vectors // 4), top_w0.shape[0]), top_w0.dtype)
    j, i = np.tril_indices(vectors, k=-1)
    top_w0z[Q * (j % 4) + i, j // 4, :] = top_w0[:, dim:].T

    arrays = {
        "dense": np.asarray(r_dense_x).reshape(P, groups, -1).transpose(2, 1, 0),
        "sparse_idx": np.asarray(r_sparse_idx),
        "emb": np.asarray(L0_rec_emb_tables),
        "bw0": np.asarray(L0_rec_bot_W0).T,
        "bb0": np.asarray(L0_rec_bot_b0),
        "bw1": transposed(L0_rec_bot_W1),
        "bb1": by_partition(L0_rec_bot_b1),
        "bw2": transposed(L0_rec_bot_W2),
        "bb2": np.asarray(L0_rec_bot_b2).reshape(-1, 1),
        "tw0x": top_w0[:, :dim].T,
        "tw0z": top_w0z,
        "tb0": np.asarray(L0_rec_top_b0),
        "tw1": transposed(L0_rec_top_W1),
        "tb1": by_partition(L0_rec_top_b1),
        "tw2": transposed(L0_rec_top_W2),
        "tb2": np.asarray(L0_rec_top_b2),
    }
    arrays = {f"in_{name}": np.ascontiguousarray(a) for name, a in arrays.items()}
    nc = bacc.Bacc("TRN2", target_bir_lowering=False, num_devices=1)
    args = [nc.dram_tensor(name, a.shape, mybir.dt.from_np(a.dtype), kind="ExternalInput").ap() for name, a in arrays.items()]
    out = nc.dram_tensor("out_y", (samples, 1), F32, kind="ExternalOutput").ap()
    dlrm_kernel(nc, *args, out)
    return run_bass_kernel_spmd(nc, [arrays], core_ids=[0]).results[0]["out_y"]
```
